# Optimizing a Trainium2 kernel written in Bass

```python
import numpy as np
import jax
import jax.numpy as jnp

def _softmax(x, axis=-1):
    return jax.nn.softmax(x, axis=axis)

def _gelu(x):
    return jax.nn.gelu(x, approximate=True)

def _silu(x):
    return jax.nn.silu(x)

def _sigmoid(x):
    return jax.nn.sigmoid(x)

def _layernorm(x, axis=-1, eps=1e-05):
    m = jnp.mean(x, axis=axis, keepdims=True)
    v = jnp.var(x, axis=axis, keepdims=True)
    return (x - m) / jnp.sqrt(v + eps)

def _scatter_add(tgt, idx, src, axis=0):
    return tgt.at[idx].add(src)

def _segment_sum(src, seg, n):
    return jax.ops.segment_sum(src, seg, n)
kernel_name = 'mk_vit_tower_cls_d2_tok_img768_r4_5ca57c'

def setup_inputs(seed: int=0):
    np.random.seed(seed)
    _w = jnp.asarray

    def _rec_inputs():
        import jax
        import jax.numpy as jnp
        _rk = jax.random.key(seed)
        x = -0.00016672 + 0.999947 * jax.random.normal(jax.random.fold_in(_rk, 1), (32, 3, 96, 96), jnp.float32)
        cls_tok = 0.02 * jax.random.normal(jax.random.fold_in(_rk, 5), (1, 1, 192), jnp.float32)
        return (x, cls_tok)
    x, cls_tok = _rec_inputs()

    def _L0_tok_setup():
        import jax, jax.numpy as jnp
        import numpy as np
        P = 16
        key = jax.random.key(seed)
        k1, k2, k3 = jax.random.split(key, 3)
        B, C, H, W = (64, 3, 96, 96)
        n_embd = 192
        patch_dim = C * P * P
        x = jax.random.normal(k1, (B, C, H, W), dtype=jnp.float32)
        bound = 1.0 / np.sqrt(patch_dim)
        W_proj = jax.random.uniform(k2, (n_embd, patch_dim), minval=-bound, maxval=bound, dtype=jnp.float32)
        b_proj = jax.random.uniform(k3, (n_embd,), minval=-bound, maxval=bound, dtype=jnp.float32)
        return {'x': x, 'W_proj': W_proj, 'b_proj': b_proj}
    _L0_tok_all = _L0_tok_setup()
    _L0_tok_in = {k: v for k, v in _L0_tok_all.items() if k in ('W_proj', 'b_proj')}
    del _L0_tok_all

    def _L0_attn_setup():
        import jax, jax.numpy as jnp
        import numpy as np
        QMIN, QMAX = (-128.0, 127.0)
        BITS_S = 4
        NUM_HEADS = 12

        def fake_quant(x, scale):
            return jnp.clip(jnp.round(x / scale), QMIN, QMAX) * scale

        def int_softmax(x, scale):
            c0, c1, c2 = (0.35815147, 0.96963238, 1.0)
            b_int = jnp.floor(c1 / c0 / scale)
            c_int = jnp.floor(c2 / c0 / scale ** 2)
            x_int = x / scale
            x_int = x_int - jnp.max(x_int, axis=-1, keepdims=True)
            x0 = -0.6931
            n = 30
            x0_int = jnp.floor(x0 / scale)
            x_int = jnp.maximum(x_int, n * x0_int)
            q = jnp.floor(x_int / x0_int)
            r = x_int - x0_int * q
            z = r * (r + b_int) + c_int
            exp_int = jnp.maximum(jnp.floor(z * 2.0 ** (n - q)), 0.0)
            exp_int_sum = jnp.sum(exp_int, axis=-1, keepdims=True)
            return (exp_int, exp_int_sum)

        def log_round(x):
            big = jnp.floor(jnp.log2(x))
            return jnp.where(x - 2.0 ** big >= 2.0 ** (big - 1.0), big + 1.0, big)

        def _sym_scale(t):
            return jnp.max(jnp.abs(t)) / QMAX
        key = jax.random.key(seed)
        k1, k2, k3 = jax.random.split(key, 3)
        B, N, C, H = (64, 197, 192, NUM_HEADS)
        D = C // H
        x = jax.random.normal(k1, (B, N, C), dtype=jnp.float32)
        qkv_w = jax.random.normal(k2, (3 * C, C), dtype=jnp.float32) * 0.02
        qkv_b = jnp.zeros((3 * C,), dtype=jnp.float32)
        proj_w = jax.random.normal(k3, (C, C), dtype=jnp.float32) * 0.02
        proj_b = jnp.zeros((C,), dtype=jnp.float32)
        w_qkv_scale = _sym_scale(qkv_w)
        w_proj_scale = _sym_scale(proj_w)
        h = x @ qkv_w.T + qkv_b
        a1_scale = _sym_scale(h)
        qkv = h.reshape(B, N, 3, H, D).transpose(2, 0, 3, 1, 4)
        q, k, v = (qkv[0], qkv[1], qkv[2])
        attn = jnp.einsum('bhnd,bhmd->bhnm', q, k) * D ** (-0.5)
        attn_scale = _sym_scale(attn)
        ctx = jnp.einsum('bhnm,bhmd->bhnd', jax.nn.softmax(attn, axis=-1), v)
        ctx = ctx.transpose(0, 2, 1, 3).reshape(B, N, C)
        a2_scale = _sym_scale(ctx)
        a3_scale = _sym_scale(ctx @ proj_w.T + proj_b)
        return {'x': x, 'qkv_w': qkv_w, 'qkv_b': qkv_b, 'proj_w': proj_w, 'proj_b': proj_b, 'w_qkv_scale': w_qkv_scale, 'a1_scale': a1_scale, 'attn_scale': attn_scale, 'a2_scale': a2_scale, 'w_proj_scale': w_proj_scale, 'a3_scale': a3_scale}
    _L0_attn_all = _L0_attn_setup()
    _L0_attn_in = {k: v for k, v in _L0_attn_all.items() if k in ('qkv_w', 'qkv_b', 'proj_w', 'proj_b', 'w_qkv_scale', 'a1_scale', 'attn_scale', 'a2_scale', 'w_proj_scale', 'a3_scale')}
    del _L0_attn_all

    def _L0_ffn_setup():
        import jax, jax.numpy as jnp
        import numpy as np
        B, SEQ, D = (2, 256, 192)
        E, H = (8, 768)
        CAPACITY = 2
        key = jax.random.key(seed)
        ks = jax.random.split(key, 6)
        x = jax.random.normal(ks[0], (B, SEQ, D), dtype=jnp.float32)
        gate_weight = jax.random.normal(ks[1], (E, D), dtype=jnp.float32) * 0.006
        w1 = jax.random.normal(ks[2], (E, D, H), dtype=jnp.float32) * (1.0 / np.sqrt(D))
        b1 = jnp.zeros((E, H), dtype=jnp.float32)
        w2 = jax.random.normal(ks[3], (E, H, D), dtype=jnp.float32) * (1.0 / np.sqrt(H))
        b2 = jnp.zeros((E, D), dtype=jnp.float32)
        return {'x': x, 'gate_weight': gate_weight, 'w1': w1, 'b1': b1, 'w2': w2, 'b2': b2}
    _L0_ffn_all = _L0_ffn_setup()
    _L0_ffn_in = {k: v for k, v in _L0_ffn_all.items() if k in ('gate_weight', 'w1', 'b1', 'w2', 'b2')}
    del _L0_ffn_all

    def _L1_attn_setup():
        import jax, jax.numpy as jnp
        import numpy as np
        N_HEAD = 12
        key = jax.random.key(seed)
        ks = jax.random.split(key, 6)
        B, T, C = (8, 256, 192)
        x = jax.random.normal(ks[0], (B, T, C), dtype=jnp.float32)
        w_attn = jax.random.normal(ks[1], (C, 3 * C), dtype=jnp.float32) * 0.02
        b_attn = jnp.zeros((3 * C,), dtype=jnp.float32)
        w_proj = jax.random.normal(ks[2], (C, C), dtype=jnp.float32) * 0.02
        b_proj = jnp.zeros((C,), dtype=jnp.float32)
        rel_emb = jax.random.normal(ks[3], (2 * 256 - 1, C // N_HEAD), dtype=jnp.float32) * 0.02
        return {'x': x, 'w_attn': w_attn, 'b_attn': b_attn, 'w_proj': w_proj, 'b_proj': b_proj, 'rel_emb': rel_emb}
    _L1_attn_all = _L1_attn_setup()
    _L1_attn_in = {k: v for k, v in _L1_attn_all.items() if k in ('w_attn', 'b_attn', 'w_proj', 'b_proj', 'rel_emb')}
    del _L1_attn_all

    def _L1_ffn_setup():
        import jax, jax.numpy as jnp
        import numpy as np
        B, S, D, F, E = (4, 512, 192, 768, 8)
        key = jax.random.key(seed)
        ks = jax.random.split(key, 5)
        return {'x': jax.random.normal(ks[0], (B, S, D), dtype=jnp.float32), 'Ws': jax.random.normal(ks[1], (D, E), dtype=jnp.float32) * 0.02, 'bs': jnp.zeros((E,), dtype=jnp.float32), 'W1': jax.random.normal(ks[2], (E, D, F), dtype=jnp.float32) * 0.02, 'b1': jnp.zeros((E, F), dtype=jnp.float32), 'W2': jax.random.normal(ks[3], (E, F, D), dtype=jnp.float32) * 0.02, 'b2': jnp.zeros((E, D), dtype=jnp.float32)}
    _L1_ffn_all = _L1_ffn_setup()
    _L1_ffn_in = {k: v for k, v in _L1_ffn_all.items() if k in ('Ws', 'bs', 'W1', 'b1', 'W2', 'b2')}
    del _L1_ffn_all
    return {'x': x, 'cls_tok': cls_tok, 'L0_tok_W_proj': _L0_tok_in['W_proj'], 'L0_tok_b_proj': _L0_tok_in['b_proj'], 'L0_attn_qkv_w': _L0_attn_in['qkv_w'], 'L0_attn_qkv_b': _L0_attn_in['qkv_b'], 'L0_attn_proj_w': _L0_attn_in['proj_w'], 'L0_attn_proj_b': _L0_attn_in['proj_b'], 'L0_attn_w_qkv_scale': _L0_attn_in['w_qkv_scale'], 'L0_attn_a1_scale': _L0_attn_in['a1_scale'], 'L0_attn_attn_scale': _L0_attn_in['attn_scale'], 'L0_attn_a2_scale': _L0_attn_in['a2_scale'], 'L0_attn_w_proj_scale': _L0_attn_in['w_proj_scale'], 'L0_attn_a3_scale': _L0_attn_in['a3_scale'], 'L0_ffn_gate_weight': _L0_ffn_in['gate_weight'], 'L0_ffn_w1': _L0_ffn_in['w1'], 'L0_ffn_b1': _L0_ffn_in['b1'], 'L0_ffn_w2': _L0_ffn_in['w2'], 'L0_ffn_b2': _L0_ffn_in['b2'], 'L1_attn_w_attn': _L1_attn_in['w_attn'], 'L1_attn_b_attn': _L1_attn_in['b_attn'], 'L1_attn_w_proj': _L1_attn_in['w_proj'], 'L1_attn_b_proj': _L1_attn_in['b_proj'], 'L1_attn_rel_emb': _L1_attn_in['rel_emb'], 'L1_ffn_Ws': _L1_ffn_in['Ws'], 'L1_ffn_bs': _L1_ffn_in['bs'], 'L1_ffn_W1': _L1_ffn_in['W1'], 'L1_ffn_b1': _L1_ffn_in['b1'], 'L1_ffn_W2': _L1_ffn_in['W2'], 'L1_ffn_b2': _L1_ffn_in['b2']}

def reference(x, cls_tok, L0_tok_W_proj, L0_tok_b_proj, L0_attn_qkv_w, L0_attn_qkv_b, L0_attn_proj_w, L0_attn_proj_b, L0_attn_w_qkv_scale, L0_attn_a1_scale, L0_attn_attn_scale, L0_attn_a2_scale, L0_attn_w_proj_scale, L0_attn_a3_scale, L0_ffn_gate_weight, L0_ffn_w1, L0_ffn_b1, L0_ffn_w2, L0_ffn_b2, L1_attn_w_attn, L1_attn_b_attn, L1_attn_w_proj, L1_attn_b_proj, L1_attn_rel_emb, L1_ffn_Ws, L1_ffn_bs, L1_ffn_W1, L1_ffn_b1, L1_ffn_W2, L1_ffn_b2):
    import jax
    import jax.numpy as jnp

    def _L0_tok_ref(x, W_proj, b_proj):
        import jax, jax.numpy as jnp
        import numpy as np
        P = 16
        b, c, h, w = x.shape
        nh, nw = (h // P, w // P)
        patches = x.reshape(b, c, nh, P, nw, P)
        patches = patches.transpose(0, 2, 4, 1, 3, 5)
        patches = patches.reshape(b, nh * nw, c * P * P)
        return jnp.einsum('bnd,ed->bne', patches, W_proj) + b_proj

    def _L0_attn_ref(x, qkv_w, qkv_b, proj_w, proj_b, w_qkv_scale, a1_scale, attn_scale, a2_scale, w_proj_scale, a3_scale):
        import jax, jax.numpy as jnp
        import numpy as np
        QMIN, QMAX = (-128.0, 127.0)
        BITS_S = 4
        NUM_HEADS = 12

        def fake_quant(x, scale):
            return jnp.clip(jnp.round(x / scale), QMIN, QMAX) * scale

        def int_softmax(x, scale):
            c0, c1, c2 = (0.35815147, 0.96963238, 1.0)
            b_int = jnp.floor(c1 / c0 / scale)
            c_int = jnp.floor(c2 / c0 / scale ** 2)
            x_int = x / scale
            x_int = x_int - jnp.max(x_int, axis=-1, keepdims=True)
            x0 = -0.6931
            n = 30
            x0_int = jnp.floor(x0 / scale)
            x_int = jnp.maximum(x_int, n * x0_int)
            q = jnp.floor(x_int / x0_int)
            r = x_int - x0_int * q
            z = r * (r + b_int) + c_int
            exp_int = jnp.maximum(jnp.floor(z * 2.0 ** (n - q)), 0.0)
            exp_int_sum = jnp.sum(exp_int, axis=-1, keepdims=True)
            return (exp_int, exp_int_sum)

        def log_round(x):
            big = jnp.floor(jnp.log2(x))
            return jnp.where(x - 2.0 ** big >= 2.0 ** (big - 1.0), big + 1.0, big)

        def _sym_scale(t):
            return jnp.max(jnp.abs(t)) / QMAX
        B, N, C = x.shape
        H = NUM_HEADS
        D = C // H
        h = x @ fake_quant(qkv_w, w_qkv_scale).T + qkv_b
        h = fake_quant(h, a1_scale)
        qkv = h.reshape(B, N, 3, H, D).transpose(2, 0, 3, 1, 4)
        q, k, v = (qkv[0], qkv[1], qkv[2])
        attn = jnp.einsum('bhnd,bhmd->bhnm', q, k) * D ** (-0.5)
        attn = fake_quant(attn, attn_scale)
        exp_int, exp_int_sum = int_softmax(attn, attn_scale)
        softmax_out = jnp.round(exp_int_sum / exp_int)
        rounds = log_round(softmax_out)
        mask = rounds >= 2.0 ** BITS_S
        qlog = jnp.clip(rounds, 0.0, 2.0 ** BITS_S - 1.0)
        p = jnp.where(mask, 0.0, 2.0 ** (-qlog))
        out = jnp.einsum('bhnm,bhmd->bhnd', p, v)
        out = out.transpose(0, 2, 1, 3).reshape(B, N, C)
        out = fake_quant(out, a2_scale)
        out = out @ fake_quant(proj_w, w_proj_scale).T + proj_b
        out = fake_quant(out, a3_scale)
        return out

    def _L0_ffn_ref(x, gate_weight, w1, b1, w2, b2):
        import jax, jax.numpy as jnp
        import numpy as np
        B, SEQ, D = (2, 256, 192)
        E, H = (8, 768)
        CAPACITY = 2
        Bb, s, d = x.shape
        xf = x.reshape(-1, d)
        S = xf.shape[0]
        k = S * CAPACITY
        logits = xf @ gate_weight.T
        scores = jax.nn.softmax(logits, axis=-1).T
        vals, idx = jax.lax.top_k(scores.reshape(-1), k)
        gate = jnp.zeros((E * S,), dtype=x.dtype).at[idx].add(vals).reshape(E, S)
        h = jax.nn.gelu(jnp.einsum('sd,edh->esh', xf, w1) + b1[:, None, :], approximate=True)
        out = jnp.einsum('esh,ehd->esd', h, w2) + b2[:, None, :]
        y = jnp.einsum('es,esd->sd', gate, out)
        return y.reshape(Bb, s, d)

    def _L1_attn_ref(x, w_attn, b_attn, w_proj, b_proj, rel_emb):
        import jax, jax.numpy as jnp
        import numpy as np
        N_HEAD = 12
        b, t, c = x.shape
        h = N_HEAD
        d = c // h
        scale = d ** (-0.5)
        qkv = x @ w_attn + b_attn
        q, k, v = jnp.split(qkv, 3, axis=-1)
        split_heads = lambda z: z.reshape(b, t, h, d).transpose(0, 2, 1, 3)
        q, k, v = map(split_heads, (q, k, v))
        q = q * scale
        scores = jnp.einsum('bhid,bhjd->bhij', q, k)
        rel = rel_emb[:t]
        rel = jnp.concatenate([jnp.zeros_like(rel[:1]), rel], axis=0)[:-1]
        scores = scores + jnp.einsum('bhid,jd->bhij', q, rel)
        causal = jnp.tril(jnp.ones((t, t), dtype=bool))
        scores = jnp.where(causal, scores, -jnp.inf)
        probs = jax.nn.softmax(scores, axis=-1)
        y = jnp.einsum('bhij,bhjd->bhid', probs, v)
        y = y.transpose(0, 2, 1, 3).reshape(b, t, c)
        return y @ w_proj + b_proj

    def _L1_ffn_ref(x, Ws, bs, W1, b1, W2, b2):
        import jax, jax.numpy as jnp
        import numpy as np
        B, S, D, F, E = (4, 512, 192, 768, 8)
        b, s, d = x.shape
        xt = x.reshape(-1, d)
        logits = xt @ Ws + bs
        probs = jax.nn.softmax(logits, axis=-1)
        routes = jnp.argmax(probs, axis=-1)
        prob_max = jnp.max(probs, axis=-1)
        h = jax.nn.gelu(jnp.einsum('td,edf->etf', xt, W1) + b1[:, None, :], approximate=False)
        y = jnp.einsum('etf,efd->etd', h, W2) + b2[:, None, :]
        out = jnp.take_along_axis(y, routes[None, :, None], axis=0)[0]
        out = out * prob_max[:, None]
        return out.reshape(b, s, d)
    h = _L0_tok_ref(x, L0_tok_W_proj, L0_tok_b_proj)
    h = jnp.concatenate([jnp.broadcast_to(cls_tok, (h.shape[0], 1, h.shape[2])), h], axis=1)
    h = h + _L0_attn_ref(_layernorm(h, axis=-1), L0_attn_qkv_w, L0_attn_qkv_b, L0_attn_proj_w, L0_attn_proj_b, L0_attn_w_qkv_scale, L0_attn_a1_scale, L0_attn_attn_scale, L0_attn_a2_scale, L0_attn_w_proj_scale, L0_attn_a3_scale)
    h = h + _L0_ffn_ref(_layernorm(h, axis=-1), L0_ffn_gate_weight, L0_ffn_w1, L0_ffn_b1, L0_ffn_w2, L0_ffn_b2)
    h = h + _L1_attn_ref(_layernorm(h, axis=-1), L1_attn_w_attn, L1_attn_b_attn, L1_attn_w_proj, L1_attn_b_proj, L1_attn_rel_emb)
    h = h + _L1_ffn_ref(_layernorm(h, axis=-1), L1_ffn_Ws, L1_ffn_bs, L1_ffn_W1, L1_ffn_b1, L1_ffn_W2, L1_ffn_b2)
    return h

_drawn_inputs = setup_inputs


def setup_inputs(seed=0):
    import zlib

    import numpy as np

    out = dict(_drawn_inputs(seed))
    spreads = {'L0_attn_qkv_b': (0.0, 0.1),
     'L0_attn_proj_b': (0.0, 0.1),
     'L0_ffn_b1': (0.0, 0.344),
     'L0_ffn_b2': (0.0, 0.1),
     'L1_attn_b_attn': (0.0, 0.1),
     'L1_attn_b_proj': (0.0, 0.1),
     'L1_ffn_bs': (0.0, 0.317),
     'L1_ffn_b1': (0.0, 0.8),
     'L1_ffn_b2': (0.0, 0.1)}
    factors = {'L1_attn_rel_emb': 200.0}
    for name, (base, spread) in spreads.items():
        noise = np.random.default_rng([zlib.crc32(name.encode()), seed]).standard_normal(out[name].shape)
        drawn = base * np.exp(spread * noise) if base else spread * noise
        out[name] = jnp.asarray(drawn.astype(out[name].dtype))
    for name, factor in factors.items():
        out[name] = (out[name] * factor).astype(out[name].dtype)
    return out
```

```python
import numpy as np
import concourse.bass as bass
from concourse import mybir
from contextlib import ExitStack

B, CH, IMG, P = 32, 3, 96, 16
NP = (IMG // P) ** 2
N = NP + 1
D, NH = 192, 12
DH = D // NH
TOK = B * N
NPT = B * NP
PD = CH * P * P
KP = PD // 128
NT = NPT // 128 + 1
ROWS = [128] * (NT - 1) + [B]
CK = 96
E, F = 8, 768
FT = F // 128
TOPK = TOK * 2
BC = 4
NCH = B // BC
HG = 3
NG = NH // HG
QR = HG * N
CT = BC * N
ST = BC * NG
MCH = [(0, 3, 384), (3, 3, 384), (6, 4, 416)]
EPS = 1e-5
BIG = 2.0 ** 23
POLY0, POLY1, POLY2 = 0.35815147, 0.96963238, 1.0

INS = ["patches", "w_patch", "b_patch", "cls",
       "a0_w", "a0_bqk", "a0_bv", "a0_pw", "a0_pb", "scales",
       "f0_gw", "f0_w1", "f0_b1", "f0_w2", "f0_b2",
       "a1_w", "a1_bqk", "a1_bv", "a1_pw", "a1_pb", "rel",
       "f1_gw", "f1_gb", "f1_w1", "f1_b1", "f1_w2", "f1_b2",
       "ident", "head_mask", "causal", "expert_rank"]


def build(nc, t, out):
    f32, bf16, i8, i32 = mybir.dt.float32, mybir.dt.bfloat16, mybir.dt.int8, mybir.dt.int32
    ALU, ACT, AX = mybir.AluOpType, mybir.ActivationFunctionType, mybir.AxisListType
    RADD = bass.bass_isa.ReduceOp.add
    with ExitStack() as ctx:
        def sb(name, shape, dt=f32):
            return ctx.enter_context(nc.sbuf_tensor(name, shape, dt))

        def sem(name):
            return ctx.enter_context(nc.semaphore(name))

        banks = [ctx.enter_context(nc.psum_tensor(f"bank{i}", [128, 512], f32)) for i in range(0)]
        PS = ctx.enter_context(nc.psum_tensor("psum", [128, 8, 512], f32))

        H = sb("H", [128, NT, D])
        XN = sb("XN", [128, NT, D])
        XT = sb("XT", [CK, 2, TOK])
        ident = sb("ident_s", [128, 128])
        identb = sb("identb_s", [128, 128], bf16)
        hmask = sb("hmask", [CK, 6])
        causal = sb("causal_s", [QR, N])
        erank = sb("erank", [128, E])
        stats = sb("stats", [128, NT, 6])
        mv = sb("mv", [128, NT, 2])
        rstd = sb("rstd", [128, NT])
        mhalf = sb("mhalf", [128, NT])
        vrow = {k: sb("row_" + k, [128, D]) for k in ("b_patch", "a0_bv", "a0_pb", "a1_bv", "a1_pb")}
        gate_w = [sb(f"gate_w{l}", [CK, 2, E]) for l in range(2)]
        gate_b = sb("gate_b", [128, E])
        b2 = [sb(f"b2_{l}", [E, D]) for l in range(2)]
        aw = [sb(f"aw{l}", [CK, 2, 3 * D]) for l in range(2)]
        pw = [sb(f"pw{l}", [CK, 2, D]) for l in range(2)]
        bqk = [sb(f"bqk{l}", [CK, 4]) for l in range(2)]
        rel = sb("rel_s", [CK, N])
        sc = sb("sc", [128, 6])
        cst = sb("cst", [128, 24])
        csti = sb("csti", [128, 4], i32)
        gates = sb("gates", [128, NT, E])
        gtmp = [sb(f"gtmp{i}", [128, NT, E]) for i in range(3)]
        gred = [sb(f"gred{i}", [128, NT]) for i in range(3)]
        gT = sb("gT", [E, TOK])
        cand = sb("cand", [128, 1], i32)
        thr = sb("thr", [128, 1], i32)
        bit = sb("bit", [128, 1], i32)
        cnt = sb("cnt", [128, 1])
        tot = sb("tot", [128, 1])
        W1 = [sb(f"W1_{i}", [CK, 2, F]) for i in range(2)]
        B1 = [sb(f"B1_{i}", [128, FT]) for i in range(2)]
        W2 = [sb(f"W2_{i}", [128, FT, D]) for i in range(2)]
        R1 = sb("R1", [128, 6912])
        R2 = sb("R2", [128, 4912])
        R3 = sb("R3", [128, 7600])
        patches = R1[:, :].rearrange("p (k n) -> p k n", k=KP)
        w_patch = R3[:, 0:KP * D].rearrange("p (k n) -> p k n", k=KP)
        HT = [R1[:, i * 2496:(i + 1) * 2496].rearrange("p (f n) -> p f n", f=FT) for i in range(2)]
        V1 = R1[0:N, 0:B * D].rearrange("p (b n) -> p b n", b=B)
        QK8 = R2[0:CK, 0:1184].bitcast(i8).rearrange("p (m n) -> p m n", m=4)
        QKB = R2[0:CK, 1184:3552].bitcast(bf16).rearrange("p (m n) -> p m n", m=4)
        V8 = R2[:, 3552:4320].bitcast(i8).rearrange("p (q n) -> p q n", q=B // 2)
        C8 = R2[0:CK, 4320:4912].bitcast(i8).rearrange("p (m n) -> p m n", m=2)
        QK1 = R2[0:CK, 0:4 * TOK].rearrange("p (m n) -> p m n", m=4)
        q0 = 0

        def carve(n, rows=128):
            nonlocal q0
            q0 += n
            return R3[0:rows, q0 - n:q0]
        QBD0 = [carve(CT * 6, CK).bitcast(bf16).rearrange("p (m b h n) -> p m b h n", m=2, b=BC, h=6) for _ in range(2)]
        VM0 = [carve(2 * D).bitcast(bf16).rearrange("p (q e n) -> p q e n", q=2, e=2) for _ in range(2)]
        PT0 = carve(444).bitcast(bf16).rearrange("p (q n) -> p q n", q=2)
        CB0 = carve(TOK, CK).bitcast(bf16).rearrange("p (m n) -> p m n", m=2)
        q0 = 0
        QBD1 = [carve(CT * 12, CK).rearrange("p (m b h n) -> p m b h n", m=2, b=BC, h=6) for _ in range(2)]
        PT1 = carve(BC * 444, N).rearrange("p (b n) -> p b n", b=BC)
        VM1 = [sb(f"VM1_{i}", [N, BC, 2, D]) for i in range(2)]
        C1T = sb("C1T", [CK, 2, TOK])
        n8 = sb("n8", [QR, 2, 8 * N], i8)
        S = [sb(f"S{i}", [QR, ST, N]) for i in range(4)]
        PB = sb("PB", [QR, ST, N], bf16)
        mx = sb("mx", [QR, ST])
        sm = sb("sm", [QR, ST])
        pwb = sb("pwb", [CK, 2, D], bf16)
        awi = sb("awi", [CK, 2, 3 * D], i8)
        pwi = sb("pwi", [CK, 2, D], i8)

        names = ("ld_const ld_small ld_patch ld_h ld_aw ld_scale embed_done embed_acc "
                 "cst_ready wq_ready identb_ready mem_ready out_done dve").split()
        s = {n: sem(n) for n in names}
        L = [{n: sem(f"{n}_{l}") for n in
              ("qk_done qk_evac v_done v_evac k_ready qbd_ready scores_done n_ready p_ready exp_done s_ready "
               "pt_done pt_act pt_dve ctx_done ctx_evac ctx_ready proj_done proj_acc "
               "logit_done lg_ready gexp gates_ready gt_done gt_ready gb_done acc_done "
               "w_loaded0 w_loaded1 up_done gelu_done down_done cnt_ready tot_ready").split()} for l in range(2)]
        LN = [{n: sem(f"ln_{n}_{l}") for n in "var pow xn tr evac_a evac_d".split()} for l in range(4)]

        PT0P = PS[:, 4, :].bitcast(bf16)[:, 0:2 * NG * 112].rearrange("p (g n) -> p g n", n=112)
        block = ctx.enter_context(nc.Block())

        def row(ap):
            return ap.partition_broadcast(128)

        NSMALL = 14

        (R_WQ, R_A1, R_AT, R_A2, R_PW, R_A3, AL_QKV, AL_S, AL_C, AL_P, X0, X30, NRQ, BQ, BI, CI, V0, V1c, V2,
         T0) = range(20)

        @block.sync
        def _(sp):
            sp.dma_start(sc[:], row(t["scales"])).then_inc(s["ld_scale"], 16)
            sp.dma_start(w_patch, t["w_patch"]).then_inc(s["ld_patch"], 16)
            sp.dma_start(vrow["b_patch"][:], row(t["b_patch"])).then_inc(s["ld_patch"], 16)
            for k in range(3):
                sp.dma_start(patches[:, 2 * k:2 * k + 2, :], t["patches"][:, 2 * k:2 * k + 2, :]).then_inc(s["ld_patch"], 16)
            sp.wait_ge(s["mem_ready"], 1)
            sp.dma_start(H[0:B, NT - 1, :], t["cls"].partition_broadcast(B)).then_inc(s["ld_h"], 16)
            sp.dma_start(aw[0][:], t["a0_w"]).then_inc(s["ld_aw"], 16)
            sp.dma_start(pw[0][:], t["a0_pw"]).then_inc(s["ld_aw"], 16)
            for dst, src in ((ident[:], t["ident"]), (hmask[:], t["head_mask"]), (causal[:], t["causal"]),
                             (erank[:], row(t["expert_rank"]))):
                sp.dma_start(dst, src).then_inc(s["ld_const"], 16)
            small = [(vrow[k][:], row(t[k])) for k in ("a0_bv", "a0_pb", "a1_bv", "a1_pb")]
            small += [(gate_w[0][:], t["f0_gw"]), (gate_w[1][:], t["f1_gw"]), (gate_b[:], row(t["f1_gb"])),
                      (b2[0][:], t["f0_b2"]), (b2[1][:], t["f1_b2"]),
                      (bqk[0][:], t["a0_bqk"]), (bqk[1][:], t["a1_bqk"]), (rel[:, 1:N], t["rel"]),
                      (aw[1][:], t["a1_w"]), (pw[1][:], t["a1_pw"])]
            assert len(small) == NSMALL
            for dst, src in small:
                sp.dma_start(dst, src).then_inc(s["ld_small"], 16)
            for l in range(2):
                w1, w2, wb = t[f"f{l}_w1"], t[f"f{l}_w2"], t[f"f{l}_b1"]
                for i in range(2):
                    if l == 1:
                        sp.wait_ge(L[0]["down_done"], NT + NT * (E - 1 + i))
                    sp.dma_start(W1[i][:], w1[i]).then_inc(L[l][f"w_loaded{i}"], 16)
                    sp.dma_start(W2[i][:], w2[i]).then_inc(L[l][f"w_loaded{i}"], 16)
                    sp.dma_start(B1[i][:], wb[i]).then_inc(L[l][f"w_loaded{i}"], 16)
                w1p, w2p = (w.rearrange("(q i) p a b -> q i p a b", i=2) for w in (w1, w2))
                wbp = wb.rearrange("(q i) p a -> q i p a", i=2)
                with sp.Fori(1, E // 2) as q:
                    for i in range(2):
                        sp.wait_ge(L[l]["down_done"], 2 * NT * q + NT * i)
                        sp.dma_start(W1[i][:], w1p[q, i]).then_inc(L[l][f"w_loaded{i}"], 16)
                        sp.dma_start(W2[i][:], w2p[q, i]).then_inc(L[l][f"w_loaded{i}"], 16)
                        sp.dma_start(B1[i][:], wbp[q, i]).then_inc(L[l][f"w_loaded{i}"], 16)
            for n in range(NT):
                sp.wait_ge(L[1]["acc_done"], NT * E + n + 1)
                sp.dma_start(out[128 * n:128 * n + ROWS[n], :], H[0:ROWS[n], n, :]).then_inc(s["out_done"], 16)
            sp.wait_ge(s["out_done"], 16 * NT)

        @block.gpsimd
        def _(pool):
            pool.memset(H[:, NT - 1, :], 0.0).then_inc(s["mem_ready"], 1)
            pool.memset(mhalf[:], -0.5).then_inc(s["mem_ready"], 1)
            pool.memset(V8.bitcast(i32), 0).then_inc(s["mem_ready"], 1)
            pool.memset(rel[:, 0:1], 0.0).then_inc(s["mem_ready"], 1)
            for i in range(2):
                pool.memset(VM1[i][:], 0.0).then_inc(s["mem_ready"], 1)
            pool.wait_ge(s["ld_const"], 64)
            pool.tensor_copy(identb[:], ident[:]).then_inc(s["identb_ready"], 1)

            def rsqrt(n):
                pool.wait_ge(LN[n]["var"], 1)
                pool.tensor_tensor(rstd[:], rstd[:], mhalf[:], ALU.pow).then_inc(LN[n]["pow"], 1)

            def mask_heads(o, q, c, l):
                for m in range(2):
                    x = q[:, m, CT * c:CT * (c + 1)].rearrange("p (b n) -> p b n", n=N)
                    mask = hmask[:, :].unsqueeze(2).broadcast_to([CK, 6, N])
                    pool.tensor_tensor(o[:, m, :, :, :], x.unsqueeze(2).broadcast_to([CK, BC, 6, N]),
                                       mask.unsqueeze(1).broadcast_to([CK, BC, 6, N]), ALU.mult).then_inc(l["qbd_ready"], 1)

            pool.wait_ge(s["mem_ready"], 6)
            rsqrt(0)
            l = L[0]
            pool.wait_ge(s["embed_done"], NT - 1)
            for i in range(2):
                pool.memset(VM0[i].bitcast(i32), 0).then_inc(s["mem_ready"], 1)
            pool.wait_ge(s["mem_ready"], 8)
            pool.wait_ge(l["v_evac"], 16)
            for c in range(NCH):
                if c >= 2:
                    pool.wait_ge(l["scores_done"], c - 1)
                if c == 0:
                    pool.wait_ge(l["k_ready"], 2)
                mask_heads(QBD0[c % 2], QKB, c, l)
                if c >= 2:
                    pool.wait_ge(l["ctx_done"], c - 1)
                for e in range(2):
                    o = VM0[c % 2][:, :, e, :].rearrange("p q (h two d) -> p q h two d", two=2, d=DH)
                    v = V8[:, 2 * c:2 * c + 2, :].rearrange("p q (h two d) -> p q h two d", two=2, d=DH)
                    pool.tensor_copy(o[:, :, :, e, :], v[:, :, :, e, :]).then_inc(l["qbd_ready"], 1)
            rsqrt(1)
            l = L[0]
            for i in range(30):
                pool.wait_ge(l["cnt_ready"], i + 1)
                pool.partition_all_reduce(tot[:], cnt[:], 128, RADD).then_inc(l["tot_ready"], 1)
            rsqrt(2)
            l = L[1]
            for c in range(NCH):
                if c >= 2:
                    pool.wait_ge(l["scores_done"], c - 1)
                if c == 0:
                    pool.wait_ge(l["qk_evac"], 12)
                mask_heads(QBD1[c % 2], QK1, c, l)
                if c >= 2:
                    pool.wait_ge(l["ctx_done"], c - 1)
                if c == 0:
                    pool.wait_ge(l["v_evac"], 16)
                for e in range(2):
                    o = VM1[c % 2][:, :, e, :].rearrange("p q (h two d) -> p q h two d", two=2, d=DH)
                    v = V1[:, BC * c:BC * (c + 1), :].rearrange("p q (h two d) -> p q h two d", two=2, d=DH)
                    pool.tensor_copy(o[:, :, :, e, :], v[:, :, :, e, :]).then_inc(l["qbd_ready"], 1)
            rsqrt(3)

        @block.tensor
        def _(pe):
            pe.wait_ge(s["ld_patch"], 80)
            for n in range(NT - 1):
                if n >= 2:
                    pe.wait_ge(s["embed_acc"], n - 1)
                for k in range(KP):
                    last = pe.matmul(PS[:, n % 2, 0:D], patches[:, k, 128 * n:128 * (n + 1)], w_patch[:, k, :],
                                     start=(k == 0), stop=(k == KP - 1))
                last.then_inc(s["embed_done"], 1)

            def transposes(n):
                if n == 0:
                    pe.wait_ge(s["ld_const"], 64)
                T = PS[0:CK, 2:8, :].rearrange("p (m b) n -> p m (b n)", m=2)
                for i in range(NT):
                    pe.wait_ge(LN[n]["xn"], i + 1)
                    for m in range(2):
                        last = pe.transpose(T[:, m, 128 * i:128 * i + ROWS[i]], XN[0:ROWS[i], i, CK * m:CK * (m + 1)],
                                            ident[0:ROWS[i], 0:ROWS[i]])
                    last.then_inc(LN[n]["tr"], 1)

            def qkv(a, l):
                pe.wait_ge(LN[2 * a]["evac_a"], 2)
                pe.wait_ge(LN[2 * a]["evac_d"], 2)
                if a == 0:
                    pe.wait_ge(s["wq_ready"], 1)
                else:
                    pe.wait_ge(s["ld_small"], 16 * NSMALL)
                u = 0
                for m in range(4):
                    for b0, nb in ((0, 12), (12, 12), (24, 8)):
                        if u >= 2:
                            pe.wait_ge(l["qk_evac"], u - 1)
                        for k in range(2):
                            last = pe.matmul(PS[0:CK, u % 2, 0:nb * N], aw[a][:, k, CK * m:CK * (m + 1)],
                                             XT[:, k, N * b0:N * (b0 + nb)], start=(k == 0), stop=(k == 1))
                        last.then_inc(l["qk_done"], 1)
                        u += 1

            transposes(0)
            l = L[0]
            qkv(0, l)
            for u in range(NCH):
                if u >= 2:
                    pe.wait_ge(l["v_evac"], 2 * (u - 1))
                for b in range(BC * u, BC * (u + 1)):
                    o = 64 * (b % 2)
                    for k in range(2):
                        last = pe.matmul(PS[o:o + N, 2 + u % 2, D * (b // 2 % 2):D * (b // 2 % 2 + 1)],
                                         XT[:, k, N * b:N * (b + 1)], aw[0][:, k, 2 * D:3 * D],
                                         start=(k == 0), stop=(k == 1))
                last.then_inc(l["v_done"], 1)

            def scores(c, l, q, k, base):
                pe.wait_ge(l["qbd_ready"], 4 * c + 2)
                if c == 0:
                    pe.wait_ge(l["k_ready"], 4 if k is QKB_K else 2)
                for i in range(ST):
                    b, g = i // NG, i % NG
                    m = g // 2
                    last = pe.matmul(PS[0:QR, base + i // 8, N * (i % 8):N * (i % 8 + 1)],
                                     q[:, m, b, HG * (g % 2):HG * (g % 2 + 1), :].rearrange("p h n -> p (h n)"),
                                     k[:, m, CT * c + N * b:CT * c + N * (b + 1)], start=True, stop=True)
                last.then_inc(l["scores_done"], 1)

            CT0P = PS[:, 5:7, 0:CT].rearrange("p e (m q n) -> p e m q n", m=2, q=2)
            QKB_K = QKB[:, 2:4, :]
            scores(0, l, QBD0[0], QKB_K, 0)
            for c in range(NCH):
                if c + 1 < NCH:
                    if c >= 1:
                        pe.wait_ge(l["n_ready"], c)
                    scores(c + 1, l, QBD0[(c + 1) % 2], QKB_K, 2 * ((c + 1) % 2))
                pe.wait_ge(l["p_ready"], c + 1)
                if c == 0:
                    pe.wait_ge(s["identb_ready"], 1)
                if c >= 1:
                    pe.wait_ge(l["pt_act"], c)
                    pe.wait_ge(l["pt_dve"], c)
                for i in range(ST):
                    b, g = i // NG, i % NG
                    o = 64 * (b % 2)
                    last = pe.transpose(PT0P[o:o + N, NG * (b // 2) + g, 0:QR], PB[:, i, :], identb[0:QR, 0:QR])
                last.then_inc(l["pt_done"], 1)
                pe.wait_ge(l["pt_act"], c + 1)
                pe.wait_ge(l["pt_dve"], c + 1)
                pe.wait_ge(l["qbd_ready"], 4 * c + 4)
                if c >= 1:
                    pe.wait_ge(l["ctx_evac"], 2 * c)
                for b in range(BC):
                    o = 64 * (b % 2)
                    for hp in range(NH // 2):
                        r = 32 * (hp % 3)
                        for e in range(2):
                            h = 2 * hp + e
                            last = pe.matmul(CT0P[r:r + 32, b % 2, hp // 3, b // 2, :],
                                             VM0[c % 2][o:o + N, b // 2, e, 32 * hp:32 * (hp + 1)],
                                             PT0[o:o + N, b // 2, N * h:N * (h + 1)], start=(e == 0), stop=(e == 1))
                last.then_inc(l["ctx_done"], 1)

            def project(a, l, c, w):
                pe.wait_ge(l["ctx_ready"], 2)
                for n in range(NT):
                    if n >= 2:
                        pe.wait_ge(l["proj_acc"], n - 1)
                    for k in range(2):
                        last = pe.matmul(PS[0:ROWS[n], n % 2, 0:D], c[:, k, 128 * n:128 * n + ROWS[n]], w[:, k, :],
                                         start=(k == 0), stop=(k == 1))
                    last.then_inc(l["proj_done"], 1)

            project(0, l, CB0, pwb)

            def experts(a, l):
                n = 2 * a + 1
                transposes(n)
                pe.wait_ge(LN[n]["evac_a"], 1)
                pe.wait_ge(LN[n]["evac_d"], 1)
                for i in range(NT):
                    for k in range(2):
                        last = pe.matmul(PS[0:ROWS[i], 0, E * i:E * (i + 1)], XT[:, k, 128 * i:128 * i + ROWS[i]],
                                         gate_w[a][:, k, :], start=(k == 0), stop=(k == 1))
                last.then_inc(l["logit_done"], 1)


            def all_experts(a, l):
                def bank(j, f):
                    return 4 + (FT * j + f) % 4

                def up_step(i, j, base, wl):
                    t0, _, w = MCH[j % 3]
                    if j % 3 == 0:
                        pe.wait_ge(l[f"w_loaded{i}"], wl)
                    for f in range(FT):
                        pe.wait_ge(l["gelu_done"], base + f + 1)
                        for k in range(2):
                            last = pe.matmul(PS[:, bank(j, f), 0:w], W1[i][:, k, 128 * f:128 * (f + 1)],
                                             XT[:, k, 128 * t0:128 * t0 + w], start=(k == 0), stop=(k == 1))
                        last.then_inc(l["up_done"], 1)

                def down_step(i, j, hid, tile):
                    t0, nt, _ = MCH[j % 3]
                    pe.wait_ge(l["gelu_done"], hid + FT + 4)
                    for n in range(nt):
                        rows = ROWS[t0 + n]
                        pe.wait_ge(l["acc_done"], tile + n + (NT - 3))
                        for f in range(FT):
                            last = pe.matmul(PS[0:rows, (NT * (j // 3) + t0 + n) % 4, 0:D],
                                             HT[j % 2][:, f, 128 * n:128 * n + rows], W2[i][:, f, :],
                                             start=(f == 0), stop=(f == FT - 1))
                        last.then_inc(l["down_done"], 1)

                def body(q, last_body):
                    e = 2 * q
                    for j in range(6):
                        if j < 5 or not last_body:
                            up_step((j + 1) // 3 % 2, j + 1, e * 18 + FT * (j + 1), q * 48 + 48 * ((j + 1) // 6) + 48)
                        down_step(j // 3, j, e * 18 + FT * j, e * 10 + NT * (j // 3) + MCH[j % 3][0])

                for _ in range(NT):
                    pe.nop().then_inc(l["down_done"], 1)
                up_step(0, 0, 0, 48)
                with pe.Fori(0, E // 2 - 1) as q:
                    body(q, False)
                body(E // 2 - 1, True)

            def gate_bias(l, a):
                pe.wait_ge(l["gates_ready"], 1)
                for i in range(NT):
                    last = pe.transpose(PS[0:E, 1 + i // 4, 128 * (i % 4):128 * (i % 4) + ROWS[i]], gates[0:ROWS[i], i, :],
                                        ident[0:ROWS[i], 0:ROWS[i]])
                last.then_inc(l["gt_done"], 1)
                pe.wait_ge(l["gt_ready"], 1)
                for i in range(NT):
                    if i >= 4:
                        pe.wait_ge(l["acc_done"], i - 3)
                    pe.matmul(PS[0:ROWS[i], (i + 2) % 4, 0:D], gT[:, 128 * i:128 * i + ROWS[i]], b2[a][:],
                              start=True, stop=True).then_inc(l["gb_done"], 1)

            experts(0, l)
            gate_bias(l, 0)
            all_experts(0, l)

            transposes(2)
            l = L[1]
            qkv(1, l)
            for u in range(16):
                if u >= 2:
                    pe.wait_ge(l["v_evac"], u - 1)
                for b in range(2 * u, 2 * u + 2):
                    for k in range(2):
                        last = pe.matmul(PS[0:N, 2 + u % 2, D * (b % 2):D * (b % 2 + 1)],
                                         XT[:, k, N * b:N * (b + 1)], aw[1][:, k, 2 * D:3 * D],
                                         start=(k == 0), stop=(k == 1))
                last.then_inc(l["v_done"], 1)
            scores(0, l, QBD1[0], QK1[:, 2:4, :], 0)
            for c in range(NCH):
                pe.wait_ge(l["p_ready"], c + 1)
                if c + 1 < NCH:
                    scores(c + 1, l, QBD1[(c + 1) % 2], QK1[:, 2:4, :], 0)
                if c >= 1:
                    pe.wait_ge(l["pt_act"], c)
                    pe.wait_ge(l["pt_dve"], c)
                for i in range(ST):
                    b, g = i // NG, i % NG
                    last = pe.transpose(PS[0:N, 2 + b, QR * g:QR * (g + 1)], S[2][:, i, :], ident[0:QR, 0:QR])
                last.then_inc(l["pt_done"], 1)
                pe.wait_ge(l["pt_act"], c + 1)
                pe.wait_ge(l["pt_dve"], c + 1)
                pe.wait_ge(l["qbd_ready"], 4 * c + 4)
                if c >= 2:
                    pe.wait_ge(l["ctx_evac"], 2 * (c - 1))
                for b in range(BC):
                    for hp in range(NH // 2):
                        r = 32 * (hp % 3)
                        for e in range(2):
                            h = 2 * hp + e
                            last = pe.matmul(PS[r:r + 32, 6 + c % 2, CT * (hp // 3) + N * b:CT * (hp // 3) + N * (b + 1)],
                                             VM1[c % 2][:, b, e, 32 * hp:32 * (hp + 1)],
                                             PT1[:, b, N * h:N * (h + 1)], start=(e == 0), stop=(e == 1))
                last.then_inc(l["ctx_done"], 1)
            project(1, l, C1T, pw[1])
            experts(1, l)
            gate_bias(l, 1)
            all_experts(1, l)

        def to_image_order(eng_copy, n, m, sem_):
            T = PS[0:CK, 2 + 3 * m:5 + 3 * m, :].rearrange("p b n -> p (b n)")
            x = XT[:, m, :].rearrange("p (b n) -> p b n", n=N)
            eng_copy(x[:, :, 1:N], T[:, 0:NPT].rearrange("p (b n) -> p b n", n=NP)).then_inc(sem_, 1)
            eng_copy(x[:, :, 0:1], T[:, NPT:TOK].unsqueeze(2)).then_inc(sem_, 1)

        def to_row_order(eng_copy, n, m, sem_):
            T = PS[0:CK, 2 + 3 * m:5 + 3 * m, :].rearrange("p b n -> p (b n)")
            eng_copy(XT[:, m, :], T[:, 0:TOK]).then_inc(sem_, 1)

        @block.scalar
        def _(act):
            def copy(o, i):
                return act.activation(o, i, ACT.Copy)

            def evacuate(n):
                act.wait_ge(LN[n]["tr"], NT)
                (to_image_order if n % 2 == 0 else to_row_order)(copy, n, 0, LN[n]["evac_a"])

            evacuate(0)
            l = L[0]
            act.wait_ge(s["cst_ready"], 1)
            act.wait_ge(s["ld_small"], 16 * NSMALL)
            u = 0
            for m in range(4):
                for b0, nb in ((0, 12), (12, 12), (24, 8)):
                    act.wait_ge(l["qk_done"], u + 1)
                    act.activation(QK8[:, m, N * b0:N * (b0 + nb)], PS[0:CK, u % 2, 0:nb * N], ACT.Identity,
                                   bias=bqk[0][:, m:m + 1], scale=cst[0:CK, AL_QKV:AL_QKV + 1]).then_inc(l["qk_evac"], 1)
                    u += 1
            def evac_scores(c):
                act.wait_ge(l["scores_done"], c + 1)
                if c >= 1:
                    act.wait_ge(l["s_ready"], c)
                act.activation(n8[:, :, :], PS[0:QR, 2 * (c % 2):2 * (c % 2) + 2, 0:8 * N], ACT.Identity,
                               bias=0.0, scale=cst[0:QR, AL_S:AL_S + 1]).then_inc(l["n_ready"], 1)

            evac_scores(0)
            for c in range(NCH):
                if c + 1 < NCH:
                    evac_scores(c + 1)
                act.wait_ge(l["pt_done"], c + 1)
                if c >= 1:
                    act.wait_ge(l["ctx_done"], c)
                act.activation(PT0[0:N, :, :].rearrange("p q (g n) -> p (q g) n", g=NG), PT0P[0:N, :, 0:QR], ACT.Copy).then_inc(l["pt_act"], 1)
                act.wait_ge(l["ctx_done"], c + 1)
                o = C8[:, :, CT * c:CT * (c + 1)].rearrange("p m (q e n) -> p m q e n", q=2, e=2)
                for e in range(2):
                    act.activation(o[:, :, :, e, :],
                                   PS[0:CK, 5 + e, 0:CT].rearrange("p (m q n) -> p m q n", m=2, q=2),
                                   ACT.Identity, bias=0.0, scale=cst[0:CK, AL_C:AL_C + 1]).then_inc(l["ctx_evac"], 1)

            def experts(a, l):
                n = 2 * a + 1
                evacuate(n)
                act.wait_ge(l["lg_ready"], 1)
                act.activation(gtmp[1][:], gtmp[0][:], ACT.Exp).then_inc(l["gexp"], 1)
                func = ACT.Gelu_apprx_tanh if a == 0 else ACT.Gelu
                if a == 1:
                    act.wait_ge(l["ctx_done"], NCH)
                for _ in range(4):
                    act.nop().then_inc(l["gelu_done"], 1)
                with act.Fori(0, E // 2) as q:
                    e = 2 * q
                    for j in range(6):
                        t0, _, w = MCH[j % 3]
                        act.wait_ge(l["down_done"], e * NT + NT + (-4, 0, 3, 6, 10, 13)[j])
                        for f in range(FT):
                            act.wait_ge(l["up_done"], e * 18 + FT * j + f + 1)
                            act.activation(HT[j % 2][:, f, 0:w], PS[:, 4 + (FT * j + f) % 4, 0:w], func,
                                           bias=B1[j // 3][:, f:f + 1], scale=1.0).then_inc(l["gelu_done"], 1)

            experts(0, l)
            evacuate(2)
            l = L[1]
            act.wait_ge(l["s_ready"], 1)
            u = 0
            for m in range(4):
                for b0, nb in ((0, 12), (12, 12), (24, 8)):
                    act.wait_ge(l["qk_done"], u + 1)
                    act.activation(QK1[:, m, N * b0:N * (b0 + nb)], PS[0:CK, u % 2, 0:nb * N], ACT.Identity,
                                   bias=bqk[1][:, m:m + 1], scale=0.25 if m < 2 else 1.0).then_inc(l["qk_evac"], 1)
                    u += 1
            def exp(c):
                act.wait_ge(l["n_ready"], c + 1)
                act.activation(S[1][:], S[0][:], ACT.Exp).then_inc(l["exp_done"], 1)

            def evac_p(c):
                act.wait_ge(l["pt_done"], c + 1)
                if c >= 1:
                    act.wait_ge(l["ctx_done"], c)
                act.activation(PT1[:, 0:2, :], PS[0:N, 2:4, 0:444], ACT.Copy).then_inc(l["pt_act"], 1)

            exp(0)
            for c in range(NCH):
                evac_p(c)
                if c + 1 < NCH:
                    exp(c + 1)
                act.wait_ge(l["ctx_done"], c + 1)
                ps = PS[0:CK, 6 + c % 2, 0:2 * CT].rearrange("p (m b n) -> p m b n", m=2, n=N)
                o = C1T[:, :, 0:NPT].rearrange("p m (b n) -> p m b n", n=NP)
                act.activation(o[:, :, BC * c:BC * (c + 1), :], ps[:, :, :, 1:N], ACT.Copy).then_inc(l["ctx_evac"], 1)
                act.activation(C1T[:, :, NPT + BC * c:NPT + BC * (c + 1)].unsqueeze(3), ps[:, :, :, 0:1],
                               ACT.Copy).then_inc(l["ctx_evac"], 1)
            experts(1, l)

        @block.vector
        def _(dve):
            done = [0]

            def step(ins):
                done[0] += 1
                return ins.then_inc(s["dve"], 1)

            def settle():
                dve.wait_ge(s["dve"], done[0])

            def then(ins):
                step(ins)
                settle()

            def col(i, n=128):
                return cst[0:n, i:i + 1]

            dve.wait_ge(s["ld_scale"], 16)
            then(dve.reciprocal(cst[:, 0:6], sc[:]))
            W, A1, AT, A2, PWs, A3 = (sc[:, i:i + 1] for i in range(6))
            step(dve.tensor_scalar(col(AL_QKV), W, col(R_A1), None, ALU.mult))
            step(dve.tensor_scalar(col(AL_S), A1, A1, 0.25, ALU.mult, ALU.mult) if False else
                 dve.scalar_tensor_tensor(col(AL_S), A1, 0.25, A1, ALU.mult, ALU.mult))
            step(dve.tensor_scalar(col(AL_C), A1, col(R_A2), None, ALU.mult))
            step(dve.tensor_scalar(col(AL_P), A2, PWs, None, ALU.mult))
            step(dve.tensor_scalar(col(V0), col(R_AT), -0.6931, None, ALU.mult))
            step(dve.tensor_scalar(col(V1c), col(R_AT), POLY1 / POLY0, None, ALU.mult))
            then(dve.scalar_tensor_tensor(col(V2), col(R_AT), POLY2 / POLY0, col(R_AT), ALU.mult, ALU.mult))
            step(dve.tensor_scalar(col(AL_S), col(AL_S), col(R_AT), None, ALU.mult))
            step(dve.tensor_scalar(col(AL_C), col(AL_C), 0.5, None, ALU.mult))
            step(dve.tensor_scalar(col(AL_P), col(AL_P), col(R_A3), None, ALU.mult))
            then(dve.tensor_copy(csti[:, 0:3], cst[:, V0:V0 + 3]))
            then(dve.tensor_copy(cst[:, T0:T0 + 3], csti[:, 0:3]))
            then(dve.tensor_tensor(cst[:, V0:V0 + 3], cst[:, T0:T0 + 3], cst[:, V0:V0 + 3], ALU.is_gt))
            then(dve.tensor_tensor(cst[:, T0:T0 + 3], cst[:, T0:T0 + 3], cst[:, V0:V0 + 3], ALU.subtract))
            step(dve.tensor_copy(cst[:, BI:BI + 2], cst[:, T0 + 1:T0 + 3]))
            step(dve.tensor_scalar(col(X0), col(T0), -1.0, None, ALU.mult))
            then(dve.tensor_scalar(col(X30), col(T0), 30.0, None, ALU.mult))
            then(dve.reciprocal(col(NRQ), col(T0)))
            then(dve.tensor_scalar(col(BQ), col(NRQ), -0.5, -0.5, ALU.mult, ALU.add))
            dve.wait_ge(s["ld_aw"], 32)
            dve.wait_ge(s["ld_small"], 16 * NSMALL)
            step(dve.tensor_scalar(awi[:], aw[0][:], col(R_WQ, CK), None, ALU.mult))
            step(dve.tensor_scalar(bqk[0][:], bqk[0][:], col(R_A1, CK), None, ALU.mult))
            step(dve.tensor_scalar(vrow["a0_bv"][:], vrow["a0_bv"][:], col(R_A1), None, ALU.mult))
            step(dve.tensor_scalar(vrow["a0_pb"][:], vrow["a0_pb"][:], col(R_A3), None, ALU.mult))
            then(dve.tensor_scalar(pwi[:], pw[0][:], col(R_PW, CK), None, ALU.mult))
            dve.tensor_copy(pwb[:], pwi[:]).then_inc(s["cst_ready"], 1)
            dve.tensor_copy(aw[0][:], awi[:]).then_inc(s["wq_ready"], 1)
            dve.wait_ge(s["ld_patch"], 80)
            for n in range(NT - 1):
                dve.wait_ge(s["embed_done"], n + 1)
                dve.tensor_tensor(H[:, n, :], PS[:, n % 2, 0:D], vrow["b_patch"][:], ALU.add).then_inc(s["embed_acc"], 1)

            def layernorm(n):
                for i in range(NT):
                    if n == 0:
                        dve.wait_ge(s["embed_acc"], min(i + 1, NT - 1))
                        if i == NT - 1:
                            dve.wait_ge(s["ld_h"], 16)
                    elif n % 2 == 1:
                        dve.wait_ge(L[n // 2]["proj_acc"], i + 1)
                    else:
                        dve.wait_ge(L[0]["acc_done"], NT * E + i + 1)
                    step(dve.bn_stats(stats[:, i, :], H[:, i, :]))
                settle()
                for i in range(NT):
                    step(dve.bn_aggr(mv[:, i, :], stats[:, i, :]))
                settle()
                dve.tensor_scalar(rstd[:], mv[:, :, 1], EPS, None, ALU.add).then_inc(LN[n]["var"], 1)
                dve.wait_ge(LN[n]["pow"], 1)
                if n:
                    dve.wait_ge(LN[n - 1]["tr"], NT)
                for i in range(NT):
                    dve.tensor_scalar(XN[:, i, :], H[:, i, :], mv[:, i, 0:1], rstd[:, i:i + 1],
                                      ALU.subtract, ALU.mult).then_inc(LN[n]["xn"], 1)
                dve.wait_ge(LN[n]["tr"], NT)
                (to_image_order if n % 2 == 0 else to_row_order)(dve.tensor_copy, n, 1, LN[n]["evac_d"])

            layernorm(0)
            l = L[0]
            dve.wait_ge(s["mem_ready"], 8)
            for u in range(NCH):
                dve.wait_ge(l["v_done"], u + 1)
                for o in (0, 64):
                    dve.scalar_tensor_tensor(V8[o:o + N, 2 * u:2 * u + 2, :],
                                             PS[o:o + N, 2 + u % 2, 0:2 * D].rearrange("p (q n) -> p q n", q=2),
                                             col(AL_QKV)[o:o + N, :],
                                             vrow["a0_bv"][o:o + N, :].unsqueeze(1).broadcast_to([N, 2, D]),
                                             ALU.mult, ALU.add).then_inc(l["v_evac"], 1)
            dve.wait_ge(l["qk_evac"], 12)
            for m in range(4):
                dve.tensor_copy(QKB[:, m, :], QK8[:, m, :]).then_inc(l["k_ready"], 1)
            c_ = QR
            for c in range(NCH):
                n3 = n8[:, :, :].rearrange("p a (i n) -> p (a i) n", n=N)
                dve.wait_ge(l["n_ready"], c + 1)
                then(dve.tensor_reduce(mx[:], n3, AX.X, ALU.max))
                dve.tensor_tensor(S[0][:], n3, mx[:, :].unsqueeze(2).broadcast_to([QR, ST, N]),
                                  ALU.subtract).then_inc(l["s_ready"], 1)
                dve.wait_ge(l["s_ready"], c + 1)
                then(dve.tensor_scalar(S[0][:], S[0][:], col(X30, c_), None, ALU.max))
                then(dve.tensor_scalar(S[1][:].bitcast(i32), S[0][:], col(NRQ, c_), col(BQ, c_), ALU.mult, ALU.add))
                step(dve.scalar_tensor_tensor(S[2][:], S[1][:].bitcast(i32), col(X0, c_), S[0][:], ALU.mult, ALU.add))
                then(dve.tensor_scalar(S[3][:].bitcast(i32), S[1][:].bitcast(i32), -BIG, 157.0 * BIG, ALU.mult, ALU.add))
                then(dve.scalar_tensor_tensor(S[0][:], S[2][:], col(BI, c_), S[2][:], ALU.add, ALU.mult))
                then(dve.scalar_tensor_tensor(S[1][:], S[0][:], col(CI, c_), S[3][:], ALU.add, ALU.mult))
                step(dve.tensor_reduce(sm[:], S[1][:], AX.X, ALU.add))
                then(dve.reciprocal(S[2][:], S[1][:]))
                then(dve.tensor_tensor(S[0][:], S[2][:], sm[:, :].unsqueeze(2).broadcast_to([QR, ST, N]), ALU.mult))
                then(dve.tensor_scalar(S[0][:], S[0][:], BIG, -BIG, ALU.add, ALU.add))
                then(dve.tensor_scalar(S[1][:], S[0][:], 4.0 / 3.0, None, ALU.mult))
                then(dve.tensor_scalar(S[2][:].bitcast(i32), S[1][:].bitcast(i32), 0x7F800000, 0x7F800000,
                                       ALU.bitwise_xor, ALU.bitwise_and))
                if c >= 1:
                    dve.wait_ge(l["pt_done"], c)
                dve.scalar_tensor_tensor(PB[:], S[2][:], 2.0 ** -14, S[2][:], ALU.is_ge, ALU.mult).then_inc(l["p_ready"], 1)
                dve.wait_ge(l["pt_done"], c + 1)
                if c >= 1:
                    dve.wait_ge(l["ctx_done"], c)
                dve.tensor_copy(PT0[64:64 + N, :, :].rearrange("p q (g n) -> p (q g) n", g=NG), PT0P[64:64 + N, :, 0:QR]).then_inc(l["pt_dve"], 1)
            dve.wait_ge(l["ctx_evac"], 2 * NCH)
            c8 = C8[:, :, :].rearrange("p m (b n) -> p m b n", n=N)
            dve.tensor_copy(CB0[:, :, 0:NPT].rearrange("p m (b n) -> p m b n", n=NP), c8[:, :, :, 1:N]).then_inc(l["ctx_ready"], 1)
            dve.tensor_copy(CB0[:, :, NPT:TOK].unsqueeze(3), c8[:, :, :, 0:1]).then_inc(l["ctx_ready"], 1)
            o8 = sb("o8", [128, NT, D], i8)
            for n in range(NT):
                r = ROWS[n]
                dve.wait_ge(l["proj_done"], n + 1)
                then(dve.scalar_tensor_tensor(o8[0:r, n, :], PS[0:r, n % 2, 0:D], col(AL_P, r), vrow["a0_pb"][0:r, :],
                                              ALU.mult, ALU.add))
                dve.scalar_tensor_tensor(H[0:r, n, :], o8[0:r, n, :], sc[0:r, 5:6], H[0:r, n, :],
                                         ALU.mult, ALU.add).then_inc(l["proj_acc"], 1)

            def softmax8(l, a):
                bc = lambda x, r=128: x[:, :].unsqueeze(2).broadcast_to([128, NT, E])
                then(dve.memset(gtmp[0][:, NT - 1, :], 0.0))
                dve.wait_ge(l["logit_done"], 1)
                ps = PS[:, 0, 0:NT * E].rearrange("p (n e) -> p n e", e=E)
                for sl, r in ((slice(0, NT - 1), 128), (slice(NT - 1, NT), B)):
                    if a == 0:
                        step(dve.tensor_copy(gtmp[0][0:r, sl, :], ps[0:r, sl, :]))
                    else:
                        k = NT - 1 if r == 128 else 1
                        step(dve.tensor_tensor(gtmp[0][0:r, sl, :], ps[0:r, sl, :],
                                               gate_b[0:r, :].unsqueeze(1).broadcast_to([r, k, E]), ALU.add))
                settle()
                then(dve.tensor_reduce(gred[0][:], gtmp[0][:], AX.X, ALU.max))
                dve.tensor_tensor(gtmp[0][:], gtmp[0][:], bc(gred[0]), ALU.subtract).then_inc(l["lg_ready"], 1)
                dve.wait_ge(l["gexp"], 1)
                then(dve.tensor_reduce(gred[1][:], gtmp[1][:], AX.X, ALU.add))
                then(dve.reciprocal(gred[2][:], gred[1][:]))
                then(dve.tensor_tensor(gtmp[2][:], gtmp[1][:], bc(gred[2]), ALU.mult))

            def router0(l):
                softmax8(l, 0)
                then(dve.memset(gtmp[0][:, NT - 1, :], -1.0))
                step(dve.tensor_copy(gtmp[0][:, 0:NT - 1, :], gtmp[2][:, 0:NT - 1, :]))
                step(dve.tensor_copy(gtmp[0][0:B, NT - 1, :], gtmp[2][0:B, NT - 1, :]))
                then(dve.memset(thr[:], 0))
                for i in range(30):
                    b = 1 << (29 - i)
                    then(dve.tensor_scalar(cand[:], thr[:], b, None, ALU.bitwise_or))
                    if i:
                        dve.wait_ge(l["tot_ready"], i)
                    dve.tensor_scalar(gtmp[1][:], gtmp[0][:], cand[:].bitcast(f32), 0.0, ALU.is_ge, ALU.add,
                                      accum_out=cnt[:]).then_inc(l["cnt_ready"], 1)
                    dve.wait_ge(l["tot_ready"], i + 1)
                    then(dve.tensor_scalar(bit[:], tot[:], float(TOPK), float(b), ALU.is_ge, ALU.mult))
                    then(dve.tensor_tensor(thr[:], thr[:], bit[:], ALU.bitwise_or))
                dve.scalar_tensor_tensor(gates[:], gtmp[0][:], thr[:].bitcast(f32), gtmp[0][:],
                                         ALU.is_ge, ALU.mult).then_inc(l["gates_ready"], 1)

            def router1(l):
                softmax8(l, 1)
                bc = lambda x: x[:, :].unsqueeze(2).broadcast_to([128, NT, E])
                then(dve.tensor_reduce(gred[0][:], gtmp[2][:], AX.X, ALU.max))
                then(dve.tensor_tensor(gtmp[0][:], gtmp[2][:], bc(gred[0]), ALU.is_equal))
                then(dve.tensor_tensor(gtmp[1][:], gtmp[0][:], erank[:, :].unsqueeze(1).broadcast_to([128, NT, E]), ALU.mult))
                then(dve.tensor_reduce(gred[1][:], gtmp[1][:], AX.X, ALU.max))
                then(dve.tensor_tensor(gtmp[0][:], gtmp[1][:], bc(gred[1]), ALU.is_equal))
                dve.tensor_tensor(gates[:], gtmp[0][:], gtmp[2][:], ALU.mult).then_inc(l["gates_ready"], 1)

            def experts(a, l):
                (router0 if a == 0 else router1)(l)
                dve.wait_ge(l["gt_done"], 1)
                dve.tensor_copy(gT[:], PS[0:E, 1:4, :].rearrange("p b n -> p (b n)")[:, 0:TOK]).then_inc(l["gt_ready"], 1)
                for n in range(NT):
                    r = ROWS[n]
                    dve.wait_ge(l["gb_done"], n + 1)
                    dve.tensor_tensor(H[0:r, n, :], PS[0:r, (n + 2) % 4, 0:D], H[0:r, n, :], ALU.add).then_inc(l["acc_done"], 1)
                pairs = gates[:, :, :].rearrange("p n (q i) -> p n q i", i=2)
                with dve.Fori(0, E // 2) as q:
                    e = 2 * q
                    for j in range(2 * NT):
                        n, r = j % NT, ROWS[j % NT]
                        dve.wait_ge(l["down_done"], e * NT + NT + j + 1)
                        dve.wait_ge(l["acc_done"], e * NT + j + 1)
                        dve.scalar_tensor_tensor(H[0:r, n, :], PS[0:r, j % 4, 0:D],
                                                 pairs[0:r, n, q, j // NT:j // NT + 1], H[0:r, n, :],
                                                 ALU.mult, ALU.add).then_inc(l["acc_done"], 1)

            layernorm(1)
            experts(0, l)
            l = L[1]
            dve.tensor_scalar(bqk[1][:, 0:2], bqk[1][:, 0:2], 0.25, None, ALU.mult).then_inc(l["s_ready"], 1)
            layernorm(2)
            for u in range(16):
                dve.wait_ge(l["v_done"], u + 1)
                dve.tensor_tensor(V1[:, 2 * u:2 * u + 2, :], PS[0:N, 2 + u % 2, 0:2 * D].rearrange("p (q n) -> p q n", q=2),
                                  vrow["a1_bv"][0:N, :].unsqueeze(1).broadcast_to([N, 2, D]), ALU.add).then_inc(l["v_evac"], 1)
            dve.wait_ge(l["qk_evac"], 12)
            for m in range(2):
                k = QK1[:, 2 + m, :].rearrange("p (b n) -> p b n", n=N)
                dve.tensor_tensor(k, k, rel[:, :].unsqueeze(1).broadcast_to([CK, B, N]), ALU.add).then_inc(l["k_ready"], 1)
            bcm = lambda x: x[:, :].unsqueeze(2).broadcast_to([QR, ST, N])

            def mask_and_max(c):
                dve.wait_ge(l["scores_done"], c + 1)
                then(dve.tensor_tensor(S[3][:], PS[0:QR, 0:2, 0:8 * N].rearrange("p a (i n) -> p a i n", n=N),
                                       causal[:, :].unsqueeze(1).broadcast_to([QR, ST, N]), ALU.add))
                then(dve.tensor_reduce(mx[:], S[3][:], AX.X, ALU.max))
                if c:
                    dve.wait_ge(l["exp_done"], c)
                dve.tensor_tensor(S[0][:], S[3][:], bcm(mx), ALU.subtract).then_inc(l["n_ready"], 1)

            mask_and_max(0)
            for c in range(NCH):
                dve.wait_ge(l["exp_done"], c + 1)
                then(dve.tensor_reduce(sm[:], S[1][:], AX.X, ALU.add))
                then(dve.reciprocal(sm[:], sm[:]))
                if c:
                    dve.wait_ge(l["pt_done"], c)
                dve.tensor_tensor(S[2][:], S[1][:], bcm(sm), ALU.mult).then_inc(l["p_ready"], 1)
                dve.wait_ge(l["pt_done"], c + 1)
                if c >= 1:
                    dve.wait_ge(l["ctx_done"], c)
                dve.tensor_copy(PT1[:, 2:4, :], PS[0:N, 4:6, 0:444]).then_inc(l["pt_dve"], 1)
                if c + 1 < NCH:
                    dve.wait_ge(l["p_ready"], c + 1)
                    mask_and_max(c + 1)
            dve.wait_ge(l["ctx_evac"], 2 * NCH)
            for _ in range(2):
                dve.nop().then_inc(l["ctx_ready"], 1)
            for n in range(NT):
                r = ROWS[n]
                dve.wait_ge(l["proj_done"], n + 1)
                then(dve.tensor_tensor(H[0:r, n, :], PS[0:r, n % 2, 0:D], H[0:r, n, :], ALU.add))
                dve.tensor_tensor(H[0:r, n, :], H[0:r, n, :], vrow["a1_pb"][0:r, :], ALU.add).then_inc(l["proj_acc"], 1)
            layernorm(3)
            experts(1, l)


def layouts(x, cls_tok, **w):
    a = np.ascontiguousarray
    out = {}
    out["patches"] = a(x.reshape(B, CH, IMG // P, P, IMG // P, P).transpose(1, 3, 5, 0, 2, 4)
                       .reshape(KP, 128, NPT).transpose(1, 0, 2))
    out["w_patch"] = a(w["L0_tok_W_proj"].T.reshape(KP, 128, D).transpose(1, 0, 2))
    out["b_patch"], out["cls"] = w["L0_tok_b_proj"], cls_tok.reshape(D)
    halves = lambda m: a(m.reshape(2, CK, -1).transpose(1, 0, 2))
    out["a0_w"], out["a0_pw"] = halves(w["L0_attn_qkv_w"].T), halves(w["L0_attn_proj_w"].T)
    out["a1_w"], out["a1_pw"] = halves(w["L1_attn_w_attn"]), halves(w["L1_attn_w_proj"])
    for l, qb, pb in ((0, "L0_attn_qkv_b", "L0_attn_proj_b"), (1, "L1_attn_b_attn", "L1_attn_b_proj")):
        out[f"a{l}_bqk"] = a(w[qb][:2 * D].reshape(4, CK).T)
        out[f"a{l}_bv"], out[f"a{l}_pb"] = w[qb][2 * D:], w[pb]
    out["scales"] = np.stack([np.asarray(w["L0_attn_" + k + "_scale"]).reshape(())
                              for k in ("w_qkv", "a1", "attn", "a2", "w_proj", "a3")])
    out["rel"] = a(np.tile(w["L1_attn_rel_emb"][:N - 1].T, (CK // DH, 1)))
    for l, gw, w1, b1, w2, b2 in ((0, w["L0_ffn_gate_weight"].T, "L0_ffn_w1", "L0_ffn_b1", "L0_ffn_w2", "L0_ffn_b2"),
                                  (1, w["L1_ffn_Ws"], "L1_ffn_W1", "L1_ffn_b1", "L1_ffn_W2", "L1_ffn_b2")):
        out[f"f{l}_gw"] = halves(gw)
        out[f"f{l}_w1"] = a(w[w1].reshape(E, 2, CK, F).transpose(0, 2, 1, 3))
        out[f"f{l}_b1"] = a(w[b1].reshape(E, FT, 128).transpose(0, 2, 1))
        out[f"f{l}_w2"] = a(w[w2].reshape(E, FT, 128, D).transpose(0, 2, 1, 3))
        out[f"f{l}_b2"] = w[b2]
    out["f1_gb"] = w["L1_ffn_bs"]
    out["ident"] = np.eye(128, dtype=np.float32)
    out["head_mask"] = (np.arange(CK)[:, None] // DH == np.arange(6)[None]).astype(np.float32)
    out["causal"] = np.where(np.arange(N)[None] <= (np.arange(QR) % N)[:, None], 0, -1e30).astype(np.float32)
    out["expert_rank"] = (E - np.arange(E)).astype(np.float32)
    return out


def kernel(**inputs):
    import concourse.bacc as bacc
    from concourse.bass_utils import run_bass_kernel_spmd

    arrays = layouts(**{k: np.asarray(v) for k, v in inputs.items()})
    nc = bacc.Bacc("TRN2", target_bir_lowering=False, num_devices=1)
    t = {}
    for name in INS:
        arr = np.ascontiguousarray(arrays[name])
        t[name] = nc.dram_tensor(f"in_{name}", arr.shape, mybir.dt.from_np(arr.dtype), kind="ExternalInput").ap()
    out = nc.dram_tensor("out_h", (TOK, D), mybir.dt.float32, kind="ExternalOutput").ap()
    build(nc, t, out)
    r = run_bass_kernel_spmd(nc, [{f"in_{k}": np.ascontiguousarray(arrays[k]) for k in INS}], core_ids=[0])
    h = r.results[0]["out_h"]
    return np.concatenate([h[NPT:].reshape(B, 1, D), h[:NPT].reshape(B, NP, D)], axis=1)
```
